# Optimizing a Trainium2 kernel written in Bass

```python
import numpy as np
import jax
import jax.numpy as jnp

def _softmax(x, axis=-1):
    return jax.nn.softmax(x, axis=axis)

def _gelu(x):
    return jax.nn.gelu(x, approximate=True)

def _silu(x):
    return jax.nn.silu(x)

def _sigmoid(x):
    return jax.nn.sigmoid(x)

def _layernorm(x, axis=-1, eps=1e-05):
    m = jnp.mean(x, axis=axis, keepdims=True)
    v = jnp.var(x, axis=axis, keepdims=True)
    return (x - m) / jnp.sqrt(v + eps)

def _scatter_add(tgt, idx, src, axis=0):
    return tgt.at[idx].add(src)

def _segment_sum(src, seg, n):
    return jax.ops.segment_sum(src, seg, n)
kernel_name = 'mk_perceiver_d1_seqx_r4_cfb34f'

def setup_inputs(seed: int=0):
    np.random.seed(seed)
    _w = jnp.asarray

    def _rec_inputs():
        import jax
        import jax.numpy as jnp
        _rk = jax.random.key(seed)
        x = -0.0005207 + 1.001 * jax.random.normal(jax.random.fold_in(_rk, 1), (8, 64, 256), jnp.float32)
        _lenS = 64 - jax.random.randint(jax.random.fold_in(_rk, 7), (8,), 0, max(1, 64 // 4) + 1, jnp.int32)
        _lenS2 = 1601 - jax.random.randint(jax.random.fold_in(_rk, 8), (8,), 0, max(1, 1601 // 4) + 1, jnp.int32)
        _ctx_1024P = jax.random.normal(jax.random.fold_in(_rk, 11), (8, 16, 256), jnp.float32)
        _ctx_1024c = jax.random.dirichlet(jax.random.fold_in(_rk, 511), 0.3 * jnp.ones((16,), jnp.float32), (8, 1601))
        _ctx_1024t = jnp.einsum('bsk,bkd->bsd', _ctx_1024c, _ctx_1024P)
        _ctx_1024t = _ctx_1024t * jax.lax.rsqrt(jnp.mean(jnp.square(_ctx_1024t)) + 1e-12) * 0.953939
        ctx_1024 = -1.39393e-06 + 0.999914 * (_ctx_1024t + 0.3 * jax.random.normal(jax.random.fold_in(_rk, 611), (8, 1601, 256), jnp.float32))
        return (x, ctx_1024)
    x, ctx_1024 = _rec_inputs()

    def _L0_xattn_setup():
        import jax, jax.numpy as jnp
        import numpy as np
        DIM = 256
        HEADS = 16
        HEAD_DIM = DIM // HEADS
        SCALE = HEAD_DIM ** (-0.5)
        key = jax.random.key(seed)
        ks = jax.random.split(key, 6)
        B, Nq, Nkv = (2, 256, 512)
        s = DIM ** (-0.5)
        return {'x': jax.random.normal(ks[0], (B, Nq, DIM), jnp.float32), 'mem': jax.random.normal(ks[1], (B, Nkv, DIM), jnp.float32), 'W_kv': jax.random.normal(ks[2], (DIM, 2 * DIM), jnp.float32) * s, 'W_q': jax.random.normal(ks[3], (DIM, DIM), jnp.float32) * s, 'W_proj': jax.random.normal(ks[4], (DIM, DIM), jnp.float32) * s, 'b_proj': jax.random.normal(ks[5], (DIM,), jnp.float32) * 0.01}
    _L0_xattn_all = _L0_xattn_setup()
    _L0_xattn_in = {k: v for k, v in _L0_xattn_all.items() if k in ('W_kv', 'W_q', 'W_proj', 'b_proj')}
    del _L0_xattn_all

    def _L0_attn_setup():
        import jax, jax.numpy as jnp
        import numpy as np
        import math
        D_MODEL = 256
        LN_EPS = 1e-05

        def _layer_norm(x):
            mu = jnp.mean(x, axis=-1, keepdims=True)
            var = jnp.var(x, axis=-1, keepdims=True)
            return (x - mu) * jax.lax.rsqrt(var + LN_EPS)
        key = jax.random.key(seed)
        ks = jax.random.split(key, 5)
        B, S, D = (4, 512, D_MODEL)
        scale = 1.0 / math.sqrt(D)
        x = jax.random.normal(ks[0], (B, S, D), dtype=jnp.float32)
        Wq = jax.random.normal(ks[1], (D, D), dtype=jnp.float32) * scale
        Wk = jax.random.normal(ks[2], (D, D), dtype=jnp.float32) * scale
        Wv = jax.random.normal(ks[3], (D, D), dtype=jnp.float32) * scale
        Wo = jax.random.normal(ks[4], (D, D), dtype=jnp.float32) * scale
        b = jnp.zeros((D,), dtype=jnp.float32)
        layerscale = 0.0001 * jnp.ones((D,), dtype=jnp.float32)
        return {'x': x, 'Wq': Wq, 'bq': b, 'Wk': Wk, 'bk': b, 'Wv': Wv, 'bv': b, 'Wo': Wo, 'bo': b, 'layerscale': layerscale}
    _L0_attn_all = _L0_attn_setup()
    _L0_attn_in = {k: v for k, v in _L0_attn_all.items() if k in ('Wq', 'bq', 'Wk', 'bk', 'Wv', 'bv', 'Wo', 'bo', 'layerscale')}
    del _L0_attn_all

    def _L0_ffn_setup():
        import jax, jax.numpy as jnp
        import numpy as np
        CAPACITY_FACTOR = 0.5
        NUM_HEADS = 16
        key = jax.random.key(seed)
        ks = jax.random.split(key, 6)
        B, N, D = (4, 1024, 256)
        s = 1.0 / np.sqrt(D)
        return {'token_inputs': jax.random.normal(ks[0], (B, N, D), jnp.float32), 'Wg': jax.random.normal(ks[1], (D, 1), jnp.float32) * s, 'Wq': jax.random.normal(ks[2], (D, D), jnp.float32) * s, 'Wk': jax.random.normal(ks[3], (D, D), jnp.float32) * s, 'Wv': jax.random.normal(ks[4], (D, D), jnp.float32) * s, 'Wo': jax.random.normal(ks[5], (D, D), jnp.float32) * s}
    _L0_ffn_all = _L0_ffn_setup()
    _L0_ffn_in = {k: v for k, v in _L0_ffn_all.items() if k in ('Wg', 'Wq', 'Wk', 'Wv', 'Wo')}
    del _L0_ffn_all
    return {'x': x, 'ctx_1024': ctx_1024, 'L0_xattn_W_kv': _L0_xattn_in['W_kv'], 'L0_xattn_W_q': _L0_xattn_in['W_q'], 'L0_xattn_W_proj': _L0_xattn_in['W_proj'], 'L0_xattn_b_proj': _L0_xattn_in['b_proj'], 'L0_attn_Wq': _L0_attn_in['Wq'], 'L0_attn_bq': _L0_attn_in['bq'], 'L0_attn_Wk': _L0_attn_in['Wk'], 'L0_attn_bk': _L0_attn_in['bk'], 'L0_attn_Wv': _L0_attn_in['Wv'], 'L0_attn_bv': _L0_attn_in['bv'], 'L0_attn_Wo': _L0_attn_in['Wo'], 'L0_attn_bo': _L0_attn_in['bo'], 'L0_attn_layerscale': _L0_attn_in['layerscale'], 'L0_ffn_Wg': _L0_ffn_in['Wg'], 'L0_ffn_Wq': _L0_ffn_in['Wq'], 'L0_ffn_Wk': _L0_ffn_in['Wk'], 'L0_ffn_Wv': _L0_ffn_in['Wv'], 'L0_ffn_Wo': _L0_ffn_in['Wo']}

def reference(x, ctx_1024, L0_xattn_W_kv, L0_xattn_W_q, L0_xattn_W_proj, L0_xattn_b_proj, L0_attn_Wq, L0_attn_bq, L0_attn_Wk, L0_attn_bk, L0_attn_Wv, L0_attn_bv, L0_attn_Wo, L0_attn_bo, L0_attn_layerscale, L0_ffn_Wg, L0_ffn_Wq, L0_ffn_Wk, L0_ffn_Wv, L0_ffn_Wo):
    import jax
    import jax.numpy as jnp

    def _L0_xattn_ref(x, mem, W_kv, W_q, W_proj, b_proj):
        import jax, jax.numpy as jnp
        import numpy as np
        DIM = 256
        HEADS = 16
        HEAD_DIM = DIM // HEADS
        SCALE = HEAD_DIM ** (-0.5)
        B, Nkv, C = mem.shape
        Nq = x.shape[1]
        kv = (mem @ W_kv).reshape(B, Nkv, 2, HEADS, HEAD_DIM)
        k = kv[:, :, 0].transpose(0, 2, 1, 3)
        v = kv[:, :, 1].transpose(0, 2, 1, 3)
        q = (x @ W_q).reshape(B, Nq, HEADS, HEAD_DIM).transpose(0, 2, 1, 3)
        attn = jnp.einsum('bhqd,bhkd->bhqk', q, k) * SCALE
        attn = jax.nn.softmax(attn, axis=-1)
        out = jnp.einsum('bhqk,bhkd->bhqd', attn, v)
        out = out.transpose(0, 2, 1, 3).reshape(B, Nq, C)
        return out @ W_proj + b_proj

    def _L0_attn_ref(x, Wq, bq, Wk, bk, Wv, bv, Wo, bo, layerscale):
        import jax, jax.numpy as jnp
        import numpy as np
        import math
        D_MODEL = 256
        LN_EPS = 1e-05

        def _layer_norm(x):
            mu = jnp.mean(x, axis=-1, keepdims=True)
            var = jnp.var(x, axis=-1, keepdims=True)
            return (x - mu) * jax.lax.rsqrt(var + LN_EPS)
        B, S, D = x.shape
        q = jnp.einsum('bsd,ed->bse', x, Wq) + bq
        k = jnp.einsum('bsd,ed->bse', x, Wk) + bk
        v = jnp.einsum('bsd,ed->bse', x, Wv) + bv
        qn = _layer_norm(q)
        kn = _layer_norm(k)
        scores = jnp.einsum('bse,bte->bst', qn, kn) / jnp.sqrt(jnp.float32(D))
        attn = jax.nn.sigmoid(scores - jnp.log(jnp.float32(S)))
        out = jnp.einsum('bst,bte->bse', attn, v)
        proj = jnp.einsum('bsd,ed->bse', out, Wo) + bo
        return proj * layerscale

    def _L0_ffn_ref(token_inputs, Wg, Wq, Wk, Wv, Wo):
        import jax, jax.numpy as jnp
        import numpy as np
        CAPACITY_FACTOR = 0.5
        NUM_HEADS = 16
        B, N, D = token_inputs.shape
        C = int(N * CAPACITY_FACTOR)
        H = NUM_HEADS
        dh = D // H
        gate = jax.nn.sigmoid((token_inputs @ Wg)[..., 0])
        _, idx = jax.lax.top_k(gate, C)
        attn_in = jnp.take_along_axis(token_inputs, idx[..., None], axis=1)
        q = (attn_in @ Wq).reshape(B, C, H, dh)
        k = (attn_in @ Wk).reshape(B, C, H, dh)
        v = (attn_in @ Wv).reshape(B, C, H, dh)
        scores = jnp.einsum('bqhd,bkhd->bhqk', q, k) / jnp.sqrt(jnp.float32(dh))
        attn = jax.nn.softmax(scores, axis=-1)
        o = jnp.einsum('bhqk,bkhd->bqhd', attn, v).reshape(B, C, D) @ Wo
        gate_sel = jnp.take_along_axis(gate, idx, axis=1)
        out = jnp.zeros_like(token_inputs)
        out = out.at[jnp.arange(B)[:, None], idx].set(o * gate_sel[..., None])
        return out
    x = x + _L0_xattn_ref(_layernorm(x, axis=-1), ctx_1024, L0_xattn_W_kv, L0_xattn_W_q, L0_xattn_W_proj, L0_xattn_b_proj)
    x = x + _L0_attn_ref(_layernorm(x, axis=-1), L0_attn_Wq, L0_attn_bq, L0_attn_Wk, L0_attn_bk, L0_attn_Wv, L0_attn_bv, L0_attn_Wo, L0_attn_bo, L0_attn_layerscale)
    x = x + _L0_ffn_ref(_layernorm(x, axis=-1), L0_ffn_Wg, L0_ffn_Wq, L0_ffn_Wk, L0_ffn_Wv, L0_ffn_Wo)
    return x

_drawn_inputs = setup_inputs


def setup_inputs(seed=0):
    import zlib

    import numpy as np

    out = dict(_drawn_inputs(seed))
    spreads = {'L0_attn_bq': (0.0, 2.0),
     'L0_attn_bk': (0.0, 2.0),
     'L0_attn_bv': (0.0, 2.0),
     'L0_attn_bo': (0.0, 2.0),
     'L0_attn_layerscale': (9.999999747378752e-05, 0.6)}
    factors = {'L0_xattn_b_proj': 5.664,
     'L0_attn_Wq': 25.339,
     'L0_attn_Wk': 64.0,
     'L0_attn_Wv': 54.818,
     'L0_attn_Wo': 59.304}
    for name, (base, spread) in spreads.items():
        noise = np.random.default_rng([zlib.crc32(name.encode()), seed]).standard_normal(out[name].shape)
        drawn = base * np.exp(spread * noise) if base else spread * noise
        out[name] = jnp.asarray(drawn.astype(out[name].dtype))
    for name, factor in factors.items():
        out[name] = (out[name] * factor).astype(out[name].dtype)
    return out
```

```python
import math
from contextlib import ExitStack

import concourse.bass as bass
from concourse import mybir
import numpy as np


LAG = 3
AHEAD = 4
K_AT = [0, 1, 2, 3]
AHEAD_AT = [23, 24, 25, 25]
A_AT = [6 + k // 2 for k in range(32)]
V_AT = [(3, 3), (4, 4), (5, 5), (5, 5), (6, 6)] + [(k, k + 1) for k in range(7, 23, 2)]
V_FIRST = 6
Q_AT, M_AT, T_AT = 2, 22, 24
CTX_AT = [6, 6, 12, 18]
LATE_FIRST = True
LO_AT = [0, 1, 2, 3, 4, 5, 9, 13, 17, 21, 23, 24, 25]


def schedule(prepare=True, ahead=True):
    chunks = [(mh, c) for mh in range(2) for c in range(4)]
    steps, split = [], []

    def project(s):
        split.append(("D",) + s)
        return [s]

    def rests():
        out, split[:] = list(split), []
        return out

    for i in range(26):
        late = rests()
        units = [("A", u) for u, at in enumerate(A_AT) if at == i] if prepare else []
        steps += [("S", i)] + ([("R", i - 1)] if i > 0 else [])
        if prepare:
            steps += [("Q",)] if i == Q_AT else []
            steps += [("M",)] if i == M_AT else []
            for k, at in enumerate(K_AT):
                if at == i:
                    steps += project(("K",) + chunks[AHEAD + k] + (False,))
            if LATE_FIRST:
                steps += late
                late = []
            for kt, at in enumerate(V_AT):
                if i in at:
                    steps += [("W", kt)] if at[0] == i else []
                    if at[1] == i:
                        steps += late + project(("V", kt))
                        late = []
            steps += units[:len(units) // 2]
        steps += late
        for k, at in enumerate(AHEAD_AT):
            if ahead and at == i:
                steps += project(("K",) + chunks[k] + (True,))
        if i >= LAG:
            steps.append(("P", i - LAG))
        steps += units[len(units) // 2:]
        if prepare:
            steps += [("T",)] if i == T_AT else []
    steps.append(("R", 25))
    for i in range(26 - LAG, 26):
        steps += [("P", i)] + rests()
    steps.append(("E",))
    return steps



def preparation():
    chunks = [(mh, c) for mh in range(2) for c in range(4)]
    steps, late = [("G", 0), ("G", 1)], []
    for s in [("K",) + c + (False,) for c in chunks] + [("V", v) for v in range(V_FIRST)]:
        steps += ([("W", s[1])] if s[0] == "V" else []) + [s] + late
        late = [("D",) + s]
    steps += late + [("Q",)]
    more = [m for v in range(V_FIRST, 13) for m in (("W", v), ("V", v), ("D", "V", v))]
    more += [m for c in chunks[:AHEAD] for m in (("K",) + c + (True,), ("D", "K") + c + (True,))]
    for u in range(32):
        steps.append(("A", u))
        steps += more[len(more) * u // 32:len(more) * (u + 1) // 32]
    return steps + [("M",), ("T",)]


def perceiver_layer(nc, x, ctxT, w_kv, w_q, w_proj, vecs, w_attn, w_ffn, consts, ms_rows, out):
    f32, f16, bf16 = mybir.dt.float32, mybir.dt.float16, mybir.dt.bfloat16
    ALU, ACT, AX = mybir.AluOpType, mybir.ActivationFunctionType, mybir.AxisListType

    B, NQ, D = 8, 64, 256
    NK = ctxT.shape[3]
    H, DH = 16, 16
    HP = H // 2
    KT = -(-NK // 128)
    HALVES = 2 * KT
    EDGE = [0, 401, 801, 1201, 1601]
    UW = 401
    G_SP = 3
    UNITS = 4 * HP
    PJ_USES = 8 + KT
    NT = 4
    WS = 64.0
    MS = 4096.0
    EXP_SCALE = DH ** -0.5 / (WS * WS)
    EXP_SHIFT = 8.0
    DVE_LO = LO_AT
    POOL_LO = HALVES - len(DVE_LO)
    KD = 12
    EPS = 1e-5

    def knum(kt):
        return min(128, NK - 128 * kt)

    ctx = ExitStack()
    with ctx:
        def sb(name, shape, dt=f32):
            return ctx.enter_context(nc.sbuf_tensor(name, shape, dt))

        def sem(name):
            return ctx.enter_context(nc.semaphore(name))

        KsF = [sb(f"k_stack{i}", [128, HP * NK], f16) for i in range(2)]
        Ks = [k[:, :].rearrange("p (g k) -> p g k", g=HP) for k in KsF]
        ctx32 = [sb(f"ctx{i}", [128, 2, NK]) for i in range(2)]
        ctx_loF = [sb(f"ctx_lo{i}", [128, 2 * NK], f16) for i in range(2)]
        ctx_lo = [c[:, :].rearrange("p (c k) -> p c k", c=2) for c in ctx_loF]
        KhF, KlF = sb("k_hi", [128, 2 * NK], f16), sb("k_lo", [128, 2 * NK], f16)
        Kh, Kl = (k[:, :].rearrange("p (c k) -> p c k", c=2) for k in (KhF, KlF))
        VsF = [sb(f"v_stack{i}", [128, KT * HP * 65], f16) for i in range(2)]
        Vs = [v[:, :].rearrange("p (t g n) -> p t g n", t=KT, g=HP) for v in VsF]
        P32 = sb("probs", [128, 4, 512])
        Plo = sb("probs_lo", [128, 4, 512], f16)
        Qall = sb("q_stack_all", [128, HP, 2, B * NQ], f16)
        Qcur = [sb(f"q_stack{i}", [98, HP, 2, NQ], f16) for i in range(2)]
        attn_out = sb("attn_out", [128, B, 128])
        Wkv = sb("w_kv_hi", [128, 2, 2 * D], f16)
        Wkv_lo = sb("w_kv_lo", [128, 2, 2 * D], f16)
        CN = sb("consts_sb", [128, consts.shape[1]])
        ident = CN[:, 0:128]
        blk = CN[:, 128:256]
        id64 = CN[:, 256:320]
        low64 = CN[:, 320:384]
        hmask = CN[:, 384:392]
        hm2 = CN[:, 392:394]
        qmask = CN[:, 394:396]
        ident16 = sb("ident16", [128, 128], f16)
        x_sb = sb("x_rows", [128, NT, D])
        m2 = sb("unit_max", [128, HP, 4])
        mneg = sb("neg_max", [128, HP])
        mm = sb("neg_max_hilo", [128, HP, 2], f16)
        rsum = sb("rsum", [128, HP])
        vlo_part = sb("vlo_part", [128, HP, 32])
        osum = sb("osum", [128, HP, DH])
        stats = sb("stats", [128, 2 * NT, 6])
        mv = sb("mean_var", [128, 2 * NT, 2])
        epsc = sb("eps_rows", [128, 2 * NT])
        rstd = sb("rstd", [128, 2 * NT])
        half = sb("minus_half", [128, 2 * NT])

        vec = sb("vectors", [128, 7, D])
        b_proj, b_q, b_k, b_v, b_o, lscale, w_gate = (vec[:, i, :] for i in range(7))
        w_projs = sb("w_proj_sb", [128, 2, D])
        wa = sb("w_attn_sb", [128, 2, 4 * D])
        wf = sb("w_ffn_sb", [128, 2, 4 * D])

        def words(buf, at, shape):
            if len(buf.shape) > 2:
                names = " ".join("abc"[:len(buf.shape) - 1])
                flat = buf[(slice(None),) * len(buf.shape)].rearrange(f"p {names} -> p ({names})")
            else:
                flat = buf[:, :]
            if buf.dtype != f32:
                flat = flat.bitcast(f32)
            v = flat[:, at:at + math.prod(shape)]
            if len(shape) == 2:
                return v.rearrange("p (a b) -> p a b", a=shape[0])
            if len(shape) == 3:
                return v.rearrange("p (a b c) -> p a b c", a=shape[0], b=shape[1])
            if len(shape) == 4:
                return v.rearrange("p (a b c d) -> p a b c d", a=shape[0], b=shape[1], c=shape[2])
            return v

        wkv32 = words(KsF[1], 0, [2, 2 * D])
        q_hi, q_lo = (KsF[1][:, at:at + 4 * B * NQ].rearrange("p (m h n) -> p m h n", m=2, h=2)
                      for at in (2048, 10240))
        wq32 = words(KsF[1], 2560, [2, D])
        xn = words(KsF[1], 3072, [NT, D])
        xnT = words(KsF[1], 4096, [2, NT * 128])

        OT = words(KsF[0], 0, [2, B, NQ])
        x1 = words(KsF[0], 1024, [NT, D])
        xln = words(KsF[0], 2048, [NT, D])
        xT = words(KsF[0], 3072, [2, NT * 128])
        x2 = words(KsF[0], 4096, [NT, D])
        x1b = words(KsF[0], 5120, [NT, D])
        qk = words(KsF[1], 0, [NT, 2 * D])
        qkn = words(KsF[1], 2048, [NT, 2 * D])
        kT = words(KsF[1], 4096, [2, NT * 128])
        qT = words(KsF[1], 5120, [2, NT * 128])
        v2 = words(ctx32[0], 0, [NT, D])
        oT = words(ctx32[0], 1024, [2, NT * 128])
        q3T = words(ctx32[0], 2048, [2, NT * 128])
        sg = words(ctx32[1], 0, [NT, NQ])
        aT = words(ctx32[1], 256, [NT, 128])
        o3T = words(ctx32[1], 1280, [2, NT * 128])
        cmp1 = words(ctx32[1], 2304, [NT, NQ])
        cmp2 = words(ctx32[1], 2560, [NT, NQ])
        negm = words(ctx32[1], 2816, [NT, NQ])
        gsm = words(ctx32[1], 3072, [8, NT])
        diag = words(ctx32[1], 768, [NT, NQ])
        kblk = [words(KsF[1], 0, [8, NT * 128]), Qall[:, :, :, :].rearrange("p g h n -> p (g h n)").bitcast(f32)
                .rearrange("p (h n) -> p h n", h=8)]
        s3 = [words(VsF[0], 1024 * t, [H, NQ]) if t < 3 else words(VsF[1], 0, [H, NQ]) for t in range(NT)]
        pT = [words(VsF[1], 1024 + 1024 * t, [8, 128]) if t < 2 else words(P32, 1024 * (t - 2), [8, 128])
              for t in range(NT)]
        pT_lo = [Plo[:, 2 * t:2 * t + 2, :].rearrange("p a (g n) -> p (a g) n", g=4) if t < 2 else
                 KhF[:, 1024 * (t - 2):1024 * (t - 1)]
                 .rearrange("p (g n) -> p g n", g=8) for t in range(NT)]
        v3 = [(ctx_loF[0] if b < 6 else KlF)[:, 528 * (b % 6):528 * (b % 6) + 528]
              .rearrange("p (g n) -> p g n", g=8) for b in range(B)]
        max3x = [sb(f"max3_{t}", [128, H]) for t in range(NT)]
        vlo3 = sb("vlo3", [128, 4, 32])
        o3s = sb("o3s", [128, 4, 32])
        o3r = sb("o3r", [128, 4, 2])
        o3 = words(KsF[1], 4096, [NT, D])
        res = x1

        uses = ["ot0", "ot1"] + [f"x1_{t}" for t in range(NT)] + ["xT0", "xT1"]
        uses += [f"{m}_{t}" for t in range(NT) for m in ("qk", "v")] + ["qT0", "qT1", "kT0", "kT1", "s2", "oT0", "oT1"]
        uses += [f"x2_{t}" for t in range(NT)] + ["yT0", "yT1", "q3_0", "q3_1", "k3_0", "k3_1", "gate"]
        uses += [f"v3_{b}" for b in range(B)] + ["sel"]
        ffn_order = [("s", 0), ("s", 1), ("p", 0), ("s", 2), ("p", 1), ("s", 3), ("p", 2), ("p", 3)]
        for what, t in ffn_order:
            uses += [f"s3_{t}_0", f"s3_{t}_1"] if what == "s" else [f"{m}_{t}_{c}" for m in ("pT", "pv") for c in (0, 1)]
        uses += ["zT0", "zT1"] + [f"out_{t}" for t in range(NT)]

        def reader(name):
            stem, _, rest = name.partition("_")
            n = [int(r) for r in rest.split("_")] if rest else []
            at = {"x1": lambda: (x1_ready, n[0] + 1), "xT1": lambda: (xT_dve, 1), "yT1": lambda: (xT_dve, 2),
                  "v": lambda: (v2_ready, n[0] + 1), "qT1": lambda: (qkT_dve, 1), "kT1": lambda: (qkT_dve, 2),
                  "s2": lambda: (sg_ready, 2), "oT1": lambda: (oT_dve, 1), "x2": lambda: (x2_ready, n[0] + 1),
                  "gate": lambda: (diag_ready, 2), "v3": lambda: (v3_ready, 2 * n[0] + 2),
                  "sel": lambda: (s3_max, 1), "s3": lambda: (s3_max, n[0] + 1),
                  "pT": lambda: (pT_ready, 2 * n[0] + n[1] + 1), "pv": lambda: (o3_ready, 2 * n[0] + n[1] + 1)}
            if stem in at:
                return at[stem]()
            if name == "k3_0":
                return kblk_act, 8
            if name == "k3_1":
                return kblk_dve, 8
            own = [u for u in uses if uses.index(u) % 8 == uses.index(name) % 8 and u in plain]
            return bank_free[uses.index(name) % 8], own.index(name) + 1

        plain = ["ot0", "ot1", "xT0", "yT0", "qT0", "kT0", "oT0", "q3_0", "q3_1", "zT0"] + [f"qk_{t}" for t in range(NT)]

        def done_by(stem, k):
            return reader(f"{stem}{k}")

        def use_bank(name):
            return ring[uses.index(name) % 8]

        bank = [ctx.enter_context(nc.psum_tensor(f"bank{i}", [128, 512], f32)) for i in range(2)]
        acc2 = ctx.enter_context(nc.psum_tensor("acc_banks", [128, 2, 512], f32))
        ab2 = ctx.enter_context(nc.psum_tensor("max_banks", [128, 2, 512], f32))
        pjb = [ctx.enter_context(nc.psum_tensor(f"pj{i}", [128, 512], f32)) for i in range(2)]
        ring = [bank[0][:, :], bank[1][:, :], acc2[:, 0, :], acc2[:, 1, :], ab2[:, 0, :], ab2[:, 1, :],
                pjb[0][:, :], pjb[1][:, :]]

        ld_const, ld_x, ld_wkv, ld_wq = sem("ld_const"), sem("ld_x"), sem("ld_wkv"), sem("ld_wq")
        ctx_ld = [sem(f"ctx_loaded{i}") for i in range(2)]
        clo_ready, wh_ready, wl_ready = sem("clo_ready"), sem("wh_ready"), sem("wl_ready")
        fills, xb_ready, q_sp, q_pool = sem("fills"), sem("xb_ready"), sem("q_rows_sp"), sem("q_rows_pool")
        ms_ready = sem("ms_rows_ready")
        ln_step, ln_rstd, xn_ready = sem("ln_step"), sem("ln_rstd"), sem("xn_ready")
        id16_ready, xnT_ps, xnT_ready = sem("id16_ready"), sem("xnT_ps"), sem("xnT_ready")
        q_ps, qh_ready, ql_ready = sem("q_ps"), sem("qh_ready"), sem("ql_ready")
        pj_ready, hi_done, pj_free = sem("pj_ready"), sem("hi_done"), sem("pj_free")
        a_ready, a_free = sem("a_ready"), sem("a_free")
        mm_step, mm_ready, mt_ready, m_rows = sem("mm_step"), sem("mm_ready"), sem("mt_ready"), sem("m_rows")
        qcur_ready, ks_ready = sem("qcur_ready"), [sem(f"ks_ready{i}") for i in range(2)]
        st_ready, exp_done, pv_done = sem("st_ready"), sem("exp_done"), sem("pv_done")
        lo_dve, lo_pool = sem("lo_dve"), sem("lo_pool")
        epi_step, vlo_copied, acc_free = sem("epi_step"), sem("vlo_copied"), sem("acc_free")

        attn_ready, tail_ps = sem("attn_ready"), sem("tail_ps")
        bank_free = [sem(f"bank_free{i}") for i in range(8)]
        ld_vec, ld_tw, x1_free = sem("ld_vec"), sem("ld_tail_weights"), sem("x1_free")
        ot_ready, x1_ready, x1b_ready = sem("ot_ready"), sem("x1_ready"), sem("x1b_ready")
        ve_ready, rstd_ready, xln_ready = sem("var_eps_ready"), sem("rstd_ready"), sem("xln_ready")
        xT_act, xT_dve, qkn_ready, v2_ready = sem("xT_act"), sem("xT_dve"), sem("qkn_ready"), sem("v2_ready")
        qkT_act, qkT_dve, sg_ready, aT_ready = sem("qkT_act"), sem("qkT_dve"), sem("sg_ready"), sem("aT_ready")
        aT_zero, oT_act, oT_dve, x2_ready = sem("aT_zero"), sem("oT_act"), sem("oT_dve"), sem("x2_ready")
        logit_ready, ge_ready, diag_ready = sem("logit_ready"), sem("ge_ready"), sem("diag_ready")
        q3_ready, kblk_act, kblk_dve = sem("q3_ready"), sem("kblk_act"), sem("kblk_dve")
        v3hi_ready, v3_ready, v3_ones = sem("v3hi_ready"), sem("v3_ready"), sem("v3_ones")
        s3_max, s3_sub, p3_ready = sem("s3_max"), sem("s3_sub"), sem("p3_ready")
        pT_ready, pTlo_ready, vlo3_ready, o3_ready = sem("pT_ready"), sem("pTlo_ready"), sem("vlo3_ready"), sem("o3_ready")
        zT_act, zT_dve, res_ready, stored = sem("zT_act"), sem("zT_dve"), sem("res_ready"), sem("stored")
        dve_step = sem("dve_step")

        steady, first = schedule(), preparation()
        before_last, last_phase = schedule(ahead=False), schedule(prepare=False, ahead=False)

        def walk(engine, step):
            def run(steps, b, n, j):
                for s in steps:
                    ahead = s[-1] is True
                    step(s[:4] if s[0] == "D" else s[:3], b, n + 1 if ahead else n, j, j if ahead else 1 - j)

            run(first, -1, 0, 1)
            with engine.Fori(0, 3) as t:
                for j in range(2):
                    run(steady, 2 * t + j, 2 * t + j + 1, j)
            run(before_last, 6, 7, 0)
            run(last_phase, 7, None, 1)

        pj_order = [q[:3] for q in first if q[0] in ("K", "V") and q[-1] is not True]

        def pj_of(s, n, nb):
            idx = pj_order.index(s)
            return PJ_USES * n + idx, pjb[(PJ_USES * nb + idx) % 2]

        def probs_rest(eng, b, i, j, done):
            kn, g = knum(i // 2), (HALVES * j + i) % 4
            eng.wait_ge(exp_done, HALVES * b + i + 3)
            eng.tensor_tensor(out=Plo[0:kn, g, :], in0=P32[0:kn, g, :],
                              in1=P32[0:kn, g, :].bitcast(bf16)[:, 1::2], op=ALU.subtract).then_inc(done, 1)

        def query_rows(eng, g, done):
            eng.wait_ge(ql_ready, 2 * (g // 4) + 2)
            part = slice(32 * (g % 4), 32 * (g % 4) + 32)
            for row, src in ((0, q_hi), (32, q_hi), (64, q_lo)):
                eng.dma_start(Qall[row:row + 32, g, :, :], src[part, g // 4, :, :]).then_inc(done, 16)

        block = ctx.enter_context(nc.Block())

        @block.sync
        def _(sp):
            sp.dma_start(x_sb[:, :, :], x.rearrange("(t p) d -> p t d", p=128)).then_inc(ld_x, 16)
            sp.dma_start(CN[:, :], consts).then_inc(ld_const, 16)
            sp.dma_start(wkv32[:, :, :], w_kv.rearrange("(c p) n -> p c n", p=128)).then_inc(ld_wkv, 16)
            sp.dma_start(ctx32[0][:, :, :], ctxT[0].rearrange("c p k -> p c k")).then_inc(ctx_ld[0], 16)
            sp.dma_start(ctx32[1][:, :, :], ctxT[1].rearrange("c p k -> p c k")).then_inc(ctx_ld[1], 16)

            def key_operand(b, n, nb, mh):
                sp.wait_ge(pj_free, PJ_USES * n + pj_order.index(("K", mh, 3)) + 3)
                for g in range(4):
                    part = slice(32 * g, 32 * g + 32)
                    for row, src in ((0, Kh), (32, Kl), (64, Kh)):
                        sp.dma_start(Ks[nb][row:row + 32, 4 * mh + g, :],
                                     src[part, mh, :]).then_inc(ks_ready[mh], 16)

            def phase(b, n, nb, load):
                if load:
                    source = sp.snap(b + 2)
                    sp.wait_ge(pj_ready, PJ_USES * (b + 1))
                    sp.dma_start(ctx32[1 - nb][:, :, :],
                                 ctxT[bass.ds(source, 1)].rearrange("o c p k -> p (o c) k")).then_inc(ctx_ld[1 - nb], 16)
                for mh in range(2):
                    key_operand(b, n, nb, mh)

            sp.dma_start(KsF[0][96:98, :], ms_rows).then_inc(ms_ready, 16)
            for g in range(G_SP):
                query_rows(sp, g, q_sp)
            phase(-1, 0, 0, False)
            sp.wait_ge(q_sp, 48 * G_SP)
            sp.wait_ge(q_pool, 48 * (HP - G_SP))
            sp.dma_start(KsF[1][96:98, :], ms_rows).then_inc(ms_ready, 16)
            sp.dma_start(vec[:, :, :], vecs).then_inc(ld_vec, 16)
            sp.dma_start(w_projs[:, :, :], w_proj.rearrange("h p n -> p h n")).then_inc(ld_tw, 16)
            sp.dma_start(wa[:, :, :], w_attn.rearrange("(c p) n -> p c n", p=128)).then_inc(ld_tw, 16)
            sp.dma_start(wf[:, :, :], w_ffn.rearrange("(c p) n -> p c n", p=128)).then_inc(ld_tw, 16)
            with sp.Fori(0, 3) as t:
                for j in range(2):
                    phase(2 * t + j, 2 * t + j + 1, 1 - j, True)
            phase(6, 7, 1, False)
            out_rows = out.rearrange("(t p) d -> t p d", p=128)
            for t in range(NT):
                sp.wait_ge(res_ready, t + 1)
                sp.dma_start(out_rows[t], res[:, t, :]).then_inc(stored, 16)
            sp.wait_ge(stored, 16 * NT)

        @block.gpsimd
        def _(pool):
            for i in range(2):
                pool.memset(Vs[i][:, :, :, 32:33], WS).then_inc(fills, 1)
            pool.memset(epsc[:, :], EPS).then_inc(fills, 1)
            pool.memset(half[:, :], -0.5).then_inc(fills, 1)
            pool.wait_ge(fills, 4)
            pool.wait_ge(ln_step, 3)
            pool.tensor_tensor(out=rstd[:, 0:NT], in0=rstd[:, 0:NT], in1=half[:, 0:NT], op=ALU.pow).then_inc(ln_rstd, 1)
            pool.wait_ge(ctx_ld[0], 16)
            pool.tensor_tensor(out=ctx_lo[0][:, 1, :], in0=ctx32[0][:, 1, :],
                               in1=ctx32[0][:, 1, :].bitcast(bf16)[:, 1::2], op=ALU.subtract).then_inc(clo_ready, 2)
            for g in range(G_SP, HP):
                query_rows(pool, g, q_pool)
            pool.wait_ge(ctx_ld[1], 16)
            for c in range(2):
                pool.tensor_tensor(out=ctx_lo[1][:, c, :], in0=ctx32[1][:, c, :],
                                   in1=ctx32[1][:, c, :].bitcast(bf16)[:, 1::2], op=ALU.subtract).then_inc(clo_ready, 2)

            def phase(b, j, load):
                pieces = [(c, a) for c in range(2) for a in (0, 1)] if load else []
                for i in range(HALVES):
                    for _ in range(CTX_AT.count(i) if pieces else 0):
                        if len(pieces) == 4:
                            pool.wait_ge(ctx_ld[j], 8 * b + 32 if j == 0 else 8 * b + 24)
                        c, a = pieces.pop(0)
                        cols = slice(EDGE[2 * a], EDGE[2 * a + 2])
                        pool.tensor_tensor(out=ctx_lo[j][:, c, cols], in0=ctx32[j][:, c, cols],
                                           in1=ctx32[j][:, c, :].bitcast(bf16)[:, 2 * cols.start + 1:2 * cols.stop:2],
                                           op=ALU.subtract).then_inc(clo_ready, 1)
                    if i not in DVE_LO:
                        probs_rest(pool, b, i, j, lo_pool)

            with pool.Fori(0, 3) as t:
                for j in range(2):
                    phase(2 * t + j, j, True)
            phase(6, 0, False)
            phase(7, 1, False)
            pool.wait_ge(ld_vec, 16)
            pool.wait_ge(xn_ready, NT)
            for t in range(NT):
                pool.tensor_tensor(out=x_sb[:, t, :], in0=x_sb[:, t, :], in1=b_proj, op=ALU.add).then_inc(xb_ready, 1)
            pool.wait_ge(attn_ready, B)
            pool.memset(aT[:, :, :], 0.0).then_inc(aT_zero, 1)
            for b in range(B):
                pool.tensor_copy(v3[b][:, :, 32:34], hm2.unsqueeze(1).to_broadcast([128, 8, 2])).then_inc(v3_ones, 1)
            pool.tensor_tensor(out=vec[:, 4, :], in0=b_o, in1=lscale, op=ALU.mult).then_inc(x1_free, 1)
            for k, w in enumerate((NT, 2 * NT, NT)):
                pool.wait_ge(ve_ready, k + 1)
                pool.tensor_tensor(out=rstd[:, 0:w], in0=rstd[:, 0:w], in1=half[:, 0:w], op=ALU.pow)\
                    .then_inc(rstd_ready, 1)
                if k == 0:
                    pool.wait_ge(x1_free, 1)
                    pool.wait_ge(x1_ready, NT)
                    for t in range(NT):
                        pool.tensor_tensor(out=x1b[:, t, :], in0=x1[:, t, :], in1=vec[:, 4, :], op=ALU.add)\
                            .then_inc(x1b_ready, 1)
            for t in range(NT):
                pool.wait_ge(s3_max, t + 1)
                pool.tensor_tensor(out=s3[t], in0=s3[t], in1=max3x[t][:, :].unsqueeze(2).to_broadcast([128, H, NQ]),
                                   op=ALU.subtract).then_inc(s3_sub, 1)

        @block.scalar
        def _(act):
            act.dma_start(wq32[:, :, :], w_q.rearrange("(c p) n -> p c n", p=128)).then_inc(ld_wq, 16)
            act.sem_inc(exp_done, 2)
            act.wait_ge(ld_const, 16)
            act.activation(ident16[:, :], ident, ACT.Copy).then_inc(id16_ready, 1)
            act.wait_ge(ld_wkv, 16)
            act.activation(Wkv[:, :, :], wkv32[:, :, :], ACT.Copy, scale=WS).then_inc(wh_ready, 1)
            for c in range(2):
                act.wait_ge(xnT_ps, c + 1)
                act.activation(xnT[:, c, :], ring[2 + c], ACT.Copy).then_inc(xnT_ready, 1)

            def step(s, b, n, j, nb):
                if s[0] == "S":
                    i = s[1]
                    kn, g = knum(i // 2), (HALVES * j + i) % 4
                    act.wait_ge(st_ready, HALVES * b + i + 1)
                    act.wait_ge(pv_done, HALVES * b + i + 1)
                    act.activation(P32[0:kn, g, :], bank[i % 2][0:kn, :], ACT.Exp, bias=EXP_SHIFT,
                                   scale=EXP_SCALE).then_inc(exp_done, 1)
                elif s[0] == "G":
                    mh = s[1]
                    act.wait_ge(q_ps, mh + 1)
                    for h2 in range(2):
                        act.activation(q_hi[:, mh, h2, :], ring[mh], ACT.Copy, scale=qmask[:, h2:h2 + 1])\
                            .then_inc(qh_ready, 1)
                elif s[0] == "K":
                    mh, c = s[1:]
                    p, pj = pj_of(s, n, nb)
                    if (mh, c) == (0, 0) and not (isinstance(n, int) and n == 0):
                        for half_of_heads in range(2):
                            act.wait_ge(ks_ready[half_of_heads], 16 * KD * n)
                    act.wait_ge(pj_ready, p + 1)
                    act.activation(Kh[:, mh, EDGE[c]:EDGE[c + 1]], pj[:, 0:EDGE[c + 1] - EDGE[c]], ACT.Copy)\
                        .then_inc(hi_done, 1)
                elif s[0] == "V":
                    kt = s[1]
                    p, pj = pj_of(s, n, nb)
                    kn = knum(kt)
                    if kt == 0 and not (isinstance(n, int) and n == 0):
                        act.wait_ge(pv_done, HALVES * b + 4)
                    act.wait_ge(pj_ready, p + 1)
                    act.activation(Vs[nb][0:kn, kt, :, 0:32],
                                   pj[0:kn, 0:D].rearrange("p (g n) -> p g n", g=HP), ACT.Copy)\
                        .then_inc(hi_done, 1)
                elif s[0] == "Q":
                    if not (isinstance(n, int) and n == 0):
                        act.wait_ge(st_ready, HALVES * b + 1)
                    else:
                        act.wait_ge(q_sp, 48 * G_SP)
                        act.wait_ge(q_pool, 48 * (HP - G_SP))
                    act.activation(Qcur[nb][0:96, :, :, :], Qall[0:96, :, :, bass.ds(n * NQ, NQ)], ACT.Copy)\
                        .then_inc(qcur_ready, 1)
                elif s[0] == "T":
                    act.wait_ge(mt_ready, n + 1)
                    act.activation(Qcur[nb][96:98, :, :, :].rearrange("p g h q -> p (g h q)"),
                                   ab2[96:98, :, :].rearrange("p a n -> p (a n)"), ACT.Copy)\
                        .then_inc(m_rows, 1)
                elif s[0] == "E":
                    act.wait_ge(pv_done, HALVES * (b + 1) + 4)
                    act.activation(vlo_part[:, :, :].rearrange("p (a g) n -> p a g n", a=2),
                                   acc2[:, :, 0:260].rearrange("p a (g n) -> p a g n", g=4)[:, :, :, 33:65],
                                   ACT.Copy).then_inc(vlo_copied, 1)

            walk(act, step)

            def taken(name):
                act.wait_ge(tail_ps, uses.index(name) + 1)

            def gone(ins, name):
                return ins.then_inc(bank_free[uses.index(name) % 8], 1)

            for k in range(2):
                taken(f"ot{k}")
                gone(act.activation(OT[:, :, 4 * k:4 * k + 4, :].rearrange("p h b q -> p b h q"),
                                    use_bank(f"ot{k}").rearrange("p (b h q) -> p b h q", b=4, h=2), ACT.Copy), f"ot{k}")
            taken("xT0")
            gone(act.activation(xT[:, 0, :], use_bank("xT0"), ACT.Copy), "xT0")
            for name, dst in (("qT0", qT), ("kT0", kT)):
                taken(name)
                gone(act.activation(dst[:, 0, :], use_bank(name), ACT.Copy), name)
            taken("s2")
            for b2 in range(2):
                rows = slice(64 * b2, 64 * b2 + 64)
                last = act.activation(sg[rows, :, :],
                                      use_bank("s2")[rows, :].rearrange("p (t s) -> p t s", t=NT)[:, :, rows],
                                      ACT.Exp, scale=-1.0 / 16.0, bias=math.log(NQ)).then_inc(sg_ready, 1)
            taken("oT0")
            gone(act.activation(oT[:, 0, :], use_bank("oT0"), ACT.Copy), "oT0")
            taken("yT0")
            gone(act.activation(xT[:, 0, :], use_bank("yT0"), ACT.Copy), "yT0")
            act.wait_ge(logit_ready, 1)
            act.activation(gsm[:, 1, :], gsm[:, 0, :], ACT.Exp, scale=-1.0).then_inc(ge_ready, 1)
            for c in range(2):
                taken(f"q3_{c}")
                gone(act.activation(q3T[:, c, :], use_bank(f"q3_{c}"), ACT.Copy), f"q3_{c}")
            taken("k3_0")
            for h in range(8):
                act.activation(kblk[0][:, h, :], use_bank("k3_0"), ACT.Copy, scale=hmask[:, h:h + 1])\
                    .then_inc(kblk_act, 1)
            for b in range(B):
                taken(f"v3_{b}")
                src = use_bank(f"v3_{b}")[:, 0:D].rearrange("p (g n) -> p g n", g=8)
                for h2 in range(2):
                    cols = slice(16 * h2, 16 * h2 + 16)
                    act.activation(v3[b][:, :, cols], src[:, :, cols], ACT.Copy, scale=hm2[:, h2:h2 + 1])\
                        .then_inc(v3hi_ready, 1)
            for what, t in ffn_order:
                if what == "s":
                    act.wait_ge(s3_sub, t + 1)
                    act.activation(s3[t], s3[t], ACT.Exp, scale=DH ** -0.5).then_inc(p3_ready, 1)
                else:
                    for c in range(2):
                        taken(f"pT_{t}_{c}")
                        act.activation(pT[t][:, 4 * c:4 * c + 4, :],
                                       use_bank(f"pT_{t}_{c}").rearrange("p (g n) -> p g n", g=4), ACT.Copy)\
                            .then_inc(pT_ready, 1)
                    for c in range(2):
                        taken(f"pv_{t}_{c}")
                        if 2 * t + c:
                            act.wait_ge(o3_ready, 2 * t + c)
                        act.activation(vlo3[:, :, :], use_bank(f"pv_{t}_{c}")[:, 0:264]
                                       .rearrange("p (g n) -> p g n", g=4)[:, :, 34:66], ACT.Copy)\
                            .then_inc(vlo3_ready, 1)
            taken("zT0")
            gone(act.activation(o3T[:, 0, :], use_bank("zT0"), ACT.Copy), "zT0")

        @block.vector
        def _(dve):
            dve.sem_inc(pj_free, 2)
            dve.sem_inc(a_free, 2)
            dve.sem_inc(acc_free, 1)
            dve.wait_ge(ld_x, 16)
            for t in range(NT):
                last = dve.bn_stats(stats[:, t, :], x_sb[:, t, :])
            last.then_inc(ln_step, 1)
            dve.wait_ge(ln_step, 1)
            for t in range(NT):
                last = dve.bn_aggr(mv[:, t, :], stats[:, t, :])
            last.then_inc(ln_step, 1)
            dve.wait_ge(ln_step, 2)
            dve.wait_ge(fills, 4)
            dve.tensor_tensor(out=rstd[:, 0:NT], in0=mv[:, 0:NT, 1], in1=epsc[:, 0:NT], op=ALU.add)\
                .then_inc(ln_step, 1)
            dve.wait_ge(ln_rstd, 1)
            for t in range(NT):
                dve.tensor_scalar(xn[:, t, :], x_sb[:, t, :], mv[:, t, 0:1], rstd[:, t:t + 1],
                                  ALU.subtract, ALU.mult).then_inc(xn_ready, 1)
            dve.wait_ge(wh_ready, 1)
            dve.scalar_tensor_tensor(out=Wkv_lo[:, :, :], in0=wkv32[:, :, :], scalar=WS, in1=Wkv[:, :, :],
                                     op0=ALU.mult, op1=ALU.subtract).then_inc(wl_ready, 1)
            dve.wait_ge(ctx_ld[0], 16)
            dve.tensor_tensor(out=ctx_lo[0][:, 0, :], in0=ctx32[0][:, 0, :],
                              in1=ctx32[0][:, 0, :].bitcast(bf16)[:, 1::2], op=ALU.subtract).then_inc(clo_ready, 2)

            def step(s, b, n, j, nb):
                if s[0] == "R":
                    if s[1] in DVE_LO:
                        probs_rest(dve, b, s[1], j, lo_dve)
                elif s[0] == "G":
                    mh = s[1]
                    dve.wait_ge(qh_ready, 2 * mh + 2)
                    for h2 in range(2):
                        dve.scalar_tensor_tensor(out=q_lo[:, mh, h2, :], in0=ring[mh], scalar=qmask[:, h2:h2 + 1],
                                                 in1=q_hi[:, mh, h2, :], op0=ALU.mult, op1=ALU.subtract)\
                            .then_inc(ql_ready, 1)
                elif s[0] == "D":
                    s = s[1:]
                    p, pj = pj_of(s, n, nb)
                    dve.wait_ge(hi_done, p + 1)
                    if s[0] == "K":
                        mh, c = s[1:]
                        cols = slice(EDGE[c], EDGE[c + 1])
                        dve.tensor_tensor(out=Kl[:, mh, cols], in0=pj[:, 0:EDGE[c + 1] - EDGE[c]],
                                          in1=Kh[:, mh, cols], op=ALU.subtract).then_inc(pj_free, 1)
                    else:
                        kt, kn = s[1], knum(s[1])
                        V = Vs[nb]
                        dve.tensor_tensor(out=V[0:kn, kt, :, 33:65],
                                          in0=pj[0:kn, 0:D].rearrange("p (g n) -> p g n", g=HP),
                                          in1=V[0:kn, kt, :, 0:32], op=ALU.subtract).then_inc(pj_free, 1)
                elif s[0] == "A":
                    u = s[1]
                    dve.wait_ge(a_ready, UNITS * n + u + 1)
                    dve.tensor_reduce(m2[:, u // 4, u % 4:u % 4 + 1], ab2[:, u % 2, 0:UW], AX.X, ALU.max)\
                        .then_inc(a_free, 1)
                elif s[0] == "M":
                    dve.wait_ge(a_free, UNITS * (n + 1) + 2)
                    dve.tensor_reduce(mneg[:, :], m2[:, :, :], AX.X, ALU.max, negate=True).then_inc(mm_step, 1)
                    dve.wait_ge(mm_step, 2 * n + 1)
                    dve.tensor_scalar(mm[:, :, 0], mneg[:, :], 1.0 / MS, None, ALU.mult).then_inc(mm_step, 1)
                    dve.wait_ge(mm_step, 2 * n + 2)
                    dve.scalar_tensor_tensor(out=mm[:, :, 1], in0=mneg[:, :], scalar=1.0 / MS, in1=mm[:, :, 0],
                                             op0=ALU.mult, op1=ALU.subtract).then_inc(mm_ready, 1)
                elif s[0] == "E":
                    dve.wait_ge(vlo_copied, b + 1)
                    av = acc2[:, :, 0:260].rearrange("p a (g n) -> p a g n", g=4)
                    for h2 in range(2):
                        rows, cols = slice(64 * h2, 64 * h2 + 64), slice(16 * h2, 16 * h2 + 16)
                        dve.tensor_tensor(out=osum[rows, :, :].rearrange("p (a g) n -> p a g n", a=2),
                                          in0=av[rows, :, :, cols],
                                          in1=vlo_part[rows, :, cols].rearrange("p (a g) n -> p a g n", a=2),
                                          op=ALU.add).then_inc(epi_step, 1)
                    dve.reciprocal(rsum[:, :].rearrange("p (a g) -> p a g", a=2), av[:, :, :, 32])\
                        .then_inc(acc_free, 1)
                    dve.wait_ge(acc_free, b + 2)
                    dve.wait_ge(epi_step, 2 * b + 2)
                    dve.tensor_tensor(out=attn_out[:, bass.ds(b, 1), :].rearrange("p o (g n) -> p (o g) n", g=HP),
                                      in0=osum[:, :, :],
                                      in1=rsum[:, :].unsqueeze(2).to_broadcast([128, HP, DH]),
                                      op=ALU.mult).then_inc(attn_ready, 1)

            walk(dve, step)

            chain = [0]

            def link(ins):
                chain[0] += 1
                ins.then_inc(dve_step, 1)
                dve.wait_ge(dve_step, chain[0])

            def taken(name):
                dve.wait_ge(tail_ps, uses.index(name) + 1)

            def gone(ins, name):
                return ins.then_inc(bank_free[uses.index(name) % 8], 1)

            norms = [0]

            def norm(src, w, dst, done):
                for k in range(w):
                    ins = dve.bn_stats(stats[:, k, :], src(k))
                link(ins)
                for k in range(w):
                    ins = dve.bn_aggr(mv[:, k, :], stats[:, k, :])
                link(ins)
                dve.tensor_tensor(out=rstd[:, 0:w], in0=mv[:, 0:w, 1], in1=epsc[:, 0:w], op=ALU.add)\
                    .then_inc(ve_ready, 1)
                norms[0] += 1
                dve.wait_ge(rstd_ready, norms[0])
                for k in range(w):
                    dve.tensor_scalar(dst(k), src(k), mv[:, k, 0:1], rstd[:, k:k + 1], ALU.subtract, ALU.mult)\
                        .then_inc(done, 1)

            dve.wait_ge(xb_ready, NT)
            for t in range(NT):
                taken(f"x1_{t}")
                dve.tensor_tensor(out=x1[:, t, :], in0=use_bank(f"x1_{t}")[:, 0:D], in1=x_sb[:, t, :], op=ALU.add)\
                    .then_inc(x1_ready, 1)
            dve.wait_ge(x1_ready, NT)
            norm(lambda t: x1[:, t, :], NT, lambda t: xln[:, t, :], xln_ready)
            taken("xT1")
            dve.tensor_copy(xT[:, 1, :], use_bank("xT1")).then_inc(xT_dve, 1)
            for t in range(NT):
                taken(f"qk_{t}")
                gone(dve.tensor_tensor(out=qk[:, t, :], in0=use_bank(f"qk_{t}"),
                                       in1=vec[:, 1:3, :].rearrange("p a n -> p (a n)"), op=ALU.add), f"qk_{t}")
                taken(f"v_{t}")
                dve.tensor_tensor(out=v2[:, t, :], in0=use_bank(f"v_{t}")[:, 0:D], in1=b_v, op=ALU.add)\
                    .then_inc(v2_ready, 1)
            dve.wait_ge(v2_ready, NT)
            norm(lambda k: qk[:, k // 2, D * (k % 2):D * (k % 2) + D], 2 * NT,
                 lambda k: qkn[:, k // 2, D * (k % 2):D * (k % 2) + D], qkn_ready)
            for name, dst in (("qT1", qT), ("kT1", kT)):
                taken(name)
                dve.tensor_copy(dst[:, 1, :], use_bank(name)).then_inc(qkT_dve, 1)
            dve.wait_ge(sg_ready, 2)
            link(dve.tensor_scalar(sg, sg, 1.0, None, ALU.add))
            link(dve.reciprocal(sg, sg))
            dve.wait_ge(aT_zero, 1)
            for b2 in range(2):
                rows = slice(64 * b2, 64 * b2 + 64)
                dve.tensor_copy(aT[rows, :, rows], sg[rows, :, :]).then_inc(aT_ready, 1)
            taken("oT1")
            dve.tensor_copy(oT[:, 1, :], use_bank("oT1")).then_inc(oT_dve, 1)
            for t in range(NT):
                taken(f"x2_{t}")
                link(dve.tensor_tensor(out=x2[:, t, :], in0=use_bank(f"x2_{t}")[:, 0:D], in1=lscale, op=ALU.mult))
                dve.wait_ge(x1b_ready, t + 1)
                dve.tensor_tensor(out=x2[:, t, :], in0=x2[:, t, :], in1=x1b[:, t, :], op=ALU.add)\
                    .then_inc(x2_ready, 1)
            dve.wait_ge(x2_ready, NT)
            norm(lambda t: x2[:, t, :], NT, lambda t: xln[:, t, :], xln_ready)
            dve.wait_ge(xln_ready, 2 * NT)
            for t in range(NT):
                ins = dve.tensor_tensor_reduce(out=qk[:, t, 0:D], in0=xln[:, t, :], in1=w_gate, scale=1.0, scalar=0.0,
                                               op0=ALU.mult, op1=ALU.add, accum_out=gsm[:, 0, t:t + 1])
            ins.then_inc(logit_ready, 1)
            taken("yT1")
            dve.tensor_copy(xT[:, 1, :], use_bank("yT1")).then_inc(xT_dve, 1)
            dve.wait_ge(ge_ready, 1)
            link(dve.tensor_scalar(gsm[:, 1, :], gsm[:, 1, :], 1.0, None, ALU.add))
            link(dve.reciprocal(gsm[:, 2, :], gsm[:, 1, :]))

            def rows_of(v):
                return v.unsqueeze(2).to_broadcast([128, NT, NQ])

            def cols_of(m):
                return m.unsqueeze(1).to_broadcast([128, NT, NQ])

            dve.tensor_tensor(out=diag, in0=cols_of(id64), in1=rows_of(gsm[:, 2, :]), op=ALU.mult)\
                .then_inc(diag_ready, 1)
            taken("k3_1")
            for h in range(8):
                dve.tensor_scalar(kblk[1][:, h, :], use_bank("k3_1"),
                                  hmask[:, h:h + 1], None, ALU.mult).then_inc(kblk_dve, 1)
            taken("gate")
            G = use_bank("gate")[:, 0:NT * NQ].rearrange("p (t n) -> p t n", t=NT)
            link(dve.tensor_tensor(out=cmp1, in0=G, in1=cols_of(id64), op=ALU.mult))
            link(dve.tensor_reduce(gsm[:, 3, :], cmp1, AX.X, ALU.add))
            link(dve.tensor_tensor(out=cmp1, in0=G, in1=rows_of(gsm[:, 3, :]), op=ALU.is_gt))
            link(dve.tensor_tensor(out=cmp2, in0=G, in1=rows_of(gsm[:, 3, :]), op=ALU.is_equal))
            link(dve.tensor_tensor(out=cmp2, in0=cmp2, in1=cols_of(low64), op=ALU.mult))
            link(dve.tensor_tensor(out=cmp1, in0=cmp1, in1=cmp2, op=ALU.add))
            link(dve.tensor_reduce(gsm[:, 4, :], cmp1, AX.X, ALU.add))
            link(dve.tensor_scalar(gsm[:, 5, :], gsm[:, 4, :], NQ // 2 - 0.5, None, ALU.is_lt))
            link(dve.tensor_tensor(out=gsm[:, 6, :], in0=gsm[:, 5, :], in1=gsm[:, 2, :], op=ALU.mult))
            dve.tensor_tensor(out=diag, in0=cols_of(id64), in1=rows_of(gsm[:, 5, :]), op=ALU.mult)\
                .then_inc(diag_ready, 1)
            for b in range(B):
                src = use_bank(f"v3_{b}")[:, 0:D].rearrange("p (g n) -> p g n", g=8)
                dve.wait_ge(v3hi_ready, 2 * b + 2)
                for h2 in range(2):
                    cols = slice(16 * h2, 16 * h2 + 16)
                    dve.scalar_tensor_tensor(out=v3[b][:, :, 34 + 16 * h2:50 + 16 * h2], in0=src[:, :, cols],
                                             scalar=hm2[:, h2:h2 + 1], in1=v3[b][:, :, cols],
                                             op0=ALU.mult, op1=ALU.subtract).then_inc(v3_ready, 1)
            taken("sel")
            link(dve.tensor_scalar(negm, use_bank("sel")[:, 0:NT * NQ].rearrange("p (t n) -> p t n", t=NT),
                                   1e30, -1e30, ALU.mult, ALU.add))
            for what, t in ffn_order:
                if what == "s":
                    for c in range(2):
                        taken(f"s3_{t}_{c}")
                        link(dve.tensor_tensor(out=s3[t][:, 8 * c:8 * c + 8, :],
                                               in0=use_bank(f"s3_{t}_{c}").rearrange("p (h n) -> p h n", h=8),
                                               in1=negm[:, t, :].unsqueeze(1).to_broadcast([128, 8, NQ]), op=ALU.add))
                    dve.tensor_reduce(max3x[t][:, :], s3[t], AX.X, ALU.max).then_inc(s3_max, 1)
                else:
                    for c in range(2):
                        dve.wait_ge(pT_ready, 2 * t + c + 1)
                        part = pT[t][:, 4 * c:4 * c + 4, :]
                        dve.tensor_tensor(out=pT_lo[t][:, 4 * c:4 * c + 4, :], in0=part,
                                          in1=part.bitcast(bf16)[:, :, 1::2], op=ALU.subtract).then_inc(pTlo_ready, 1)
                    for c in range(2):
                        dve.wait_ge(vlo3_ready, 2 * t + c + 1)
                        av = use_bank(f"pv_{t}_{c}")[:, 0:264].rearrange("p (g n) -> p g n", g=4)
                        link(dve.tensor_tensor(out=o3s[:, :, :], in0=av[:, :, 0:32], in1=vlo3[:, :, :], op=ALU.add))
                        link(dve.reciprocal(o3r[:, :, :], av[:, :, 32:34]))
                        dve.tensor_tensor(out=o3[:, t, 128 * c:128 * c + 128].rearrange("p (g n) -> p g n", g=8),
                                          in0=o3s[:, :, :].rearrange("p g (h n) -> p (g h) n", h=2),
                                          in1=o3r[:, :, :].rearrange("p g h -> p (g h)").unsqueeze(2)
                                          .to_broadcast([128, 8, DH]),
                                          op=ALU.mult).then_inc(o3_ready, 1)
            taken("zT1")
            dve.tensor_copy(o3T[:, 1, :], use_bank("zT1")).then_inc(zT_dve, 1)
            for t in range(NT):
                taken(f"out_{t}")
                dve.scalar_tensor_tensor(out=res[:, t, :], in0=use_bank(f"out_{t}")[:, 0:D], scalar=gsm[:, 6, t:t + 1],
                                         in1=x2[:, t, :], op0=ALU.mult, op1=ALU.add).then_inc(res_ready, 1)

        @block.tensor
        def _(pe):
            pe.sem_inc(pv_done, 4)
            pe.wait_ge(ld_const, 16)
            for c in range(2):
                for t in range(NT):
                    pe.wait_ge(xn_ready, t + 1)
                    last = pe.transpose(ring[2 + c][:, 128 * t:128 * t + 128], xn[:, t, 128 * c:128 * c + 128],
                                        ident)
                last.then_inc(xnT_ps, 1)
            pe.wait_ge(xnT_ready, 2)
            pe.wait_ge(ld_wq, 16)
            def hi(nb, c, a, w):
                return ctx32[nb][:, c, :].bitcast(bf16)[:, 2 * a + 1:2 * (a + w):2]

            def step(s, b, n, j, nb):
                if s[0] == "S":
                    i = s[1]
                    kt, kn = i // 2, knum(i // 2)
                    if i == 0:
                        pe.wait_ge(m_rows, b + 1)
                        pe.wait_ge(ms_ready, 32)
                    pe.wait_ge(exp_done, HALVES * b + i + 1)
                    for q in range(4):
                        g = 4 * (i % 2) + q
                        last = pe.matmul(bank[i % 2][0:kn, 128 * q:128 * q + 128],
                                         Ks[j][0:98, g, 128 * kt:128 * kt + kn],
                                         Qcur[j][0:98, g, :, :].rearrange("p h q -> p (h q)"),
                                         start=True, stop=True)
                    last.then_inc(st_ready, 1)
                elif s[0] == "P":
                    i = s[1]
                    kt, kn, r = i // 2, knum(i // 2), (HALVES * j + i) % 4
                    if i == 0:
                        pe.wait_ge(pj_free, PJ_USES * (b + 1) + 2)
                        pe.wait_ge(acc_free, b + 1)
                    if i in DVE_LO:
                        pe.wait_ge(lo_dve, len(DVE_LO) * b + DVE_LO.index(i) + 1)
                    else:
                        pool_lo = [q for q in range(HALVES) if q not in DVE_LO]
                        pe.wait_ge(lo_pool, len(pool_lo) * b + pool_lo.index(i) + 1)
                    for q in range(4):
                        g = 4 * (i % 2) + q
                        o = acc2[:, i % 2, 65 * q:65 * q + 65]
                        pe.matmul(o, P32[0:kn, r, 128 * q:128 * q + 128].bitcast(bf16)[:, 1::2],
                                  Vs[j][0:kn, kt, g, :], start=(kt == 0 and q == 0), stop=False,
                                  skip_group_check=True)
                        last = pe.matmul(o[:, 0:33], Plo[0:kn, r, 128 * q:128 * q + 128],
                                         Vs[j][0:kn, kt, g, 0:33], start=False, stop=(kt == KT - 1),
                                         skip_group_check=True)
                    last.then_inc(pv_done, 1)
                elif s[0] == "G":
                    mh = s[1]
                    for c in range(2):
                        last = pe.matmul(ring[mh], wq32[:, c, 128 * mh:128 * mh + 128], xnT[:, c, :],
                                         start=(c == 0), stop=(c == 1))
                    last.then_inc(q_ps, 1)
                elif s[0] in "KVW":
                    p, pj = pj_of(("V", s[1]) if s[0] == "W" else s, n, nb)
                    if s == ("K", 0, 0):
                        pe.wait_ge(clo_ready, 4 * n + 4)
                        if isinstance(n, int) and n == 0:
                            pe.wait_ge(wl_ready, 1)
                    if s[0] != "V":
                        pe.wait_ge(pj_free, p + 1)
                    if s[0] == "K":
                        mh, c = s[1:]
                        a, w = EDGE[c], EDGE[c + 1] - EDGE[c]
                        mcol = slice(128 * mh, 128 * mh + 128)
                        todo = [(pj[:, 0:w], W[:, ch, mcol], m(nb, ch, a, w))
                                for ch in range(2)
                                for W, m in ((Wkv, hi), (Wkv_lo, hi),
                                             (Wkv, lambda nb, ch, a, w: ctx_lo[nb][:, ch, a:a + w]))]
                    else:
                        kt, kn = s[1], knum(s[1])
                        a = 128 * kt
                        todo = [(pj[0:kn, 0:D], m, W[:, ch, D:2 * D])
                                for ch in (range(1) if s[0] == "W" else range(1, 2))
                                for m, W in ((hi(nb, ch, a, kn), Wkv), (hi(nb, ch, a, kn), Wkv_lo),
                                             (ctx_lo[nb][:, ch, a:a + kn], Wkv))]
                    for k, (o, l, r) in enumerate(todo):
                        last = pe.matmul(o, l, r, start=(k == 0 and s[0] != "V"),
                                         stop=(k == len(todo) - 1 and s[0] != "W"))
                    if s[0] != "W":
                        last.then_inc(pj_ready, 1)
                elif s[0] == "A":
                    u = s[1]
                    g, a = u // 4, 400 * (u % 4)
                    if u == 0:
                        pe.wait_ge(qcur_ready, n + 1)
                    if u % (UNITS // 2) == 0:
                        pe.wait_ge(ks_ready[2 * u // UNITS], 16 * KD * (n + 1))
                    pe.wait_ge(a_free, UNITS * n + u + 1)
                    pe.matmul(ab2[:, u % 2, 0:UW], Qcur[nb][0:96, g, :, :].rearrange("p h q -> p (h q)"),
                              Ks[nb][0:96, g, a:a + UW], start=True, stop=True).then_inc(a_ready, 1)
                elif s[0] == "T":
                    pe.wait_ge(mm_ready, n + 1)
                    if isinstance(n, int) and n == 0:
                        pe.wait_ge(id16_ready, 1)
                    for g in range(HP):
                        last = pe.matmul(ab2[96:98, g // 4, 128 * (g % 4):128 * (g % 4) + 128], mm[:, g, :],
                                         ident16[:, :], start=(g % 4 == 0), stop=(g % 4 == 3),
                                         skip_group_check=True)
                    last.then_inc(mt_ready, 1)

            walk(pe, step)

            def begin(name):
                k = uses.index(name)
                if k >= 8:
                    wait_for, count = reader(uses[k - 8])
                    pe.wait_ge(wait_for, count)
                return use_bank(name)

            def finish(ins):
                ins.then_inc(tail_ps, 1)

            def transposed(name, src, w=NT):
                o = begin(name)
                for t in range(w):
                    last = pe.transpose(o[:, 128 * t:128 * t + 128], src(t), ident)
                finish(last)

            def product(o, pairs):
                for k, (l, r) in enumerate(pairs):
                    last = pe.matmul(o, l, r, start=(k == 0), stop=(k == len(pairs) - 1))
                return last

            tile = [slice(128 * t, 128 * t + 128) for t in range(NT)]
            pe.wait_ge(attn_ready, B)
            for k in range(2):
                transposed(f"ot{k}", lambda b: attn_out[:, 4 * k + b, :], 4)
            for k in range(2):
                pe.wait_ge(*done_by("ot", k))
            pe.wait_ge(ld_tw, 48)
            for t in range(NT):
                finish(product(begin(f"x1_{t}")[:, 0:D],
                               [(OT[:, h2, 2 * t:2 * t + 2, :].rearrange("p b q -> p (b q)"), w_projs[:, h2, :])
                                for h2 in range(2)]))
            pe.wait_ge(xln_ready, NT)
            for c in range(2):
                transposed(f"xT{c}", lambda t: xln[:, t, 128 * c:128 * c + 128])
            pe.wait_ge(*done_by("xT", 0))
            pe.wait_ge(xT_dve, 1)
            for t in range(NT):
                finish(product(begin(f"qk_{t}"), [(xT[:, c, tile[t]], wa[:, c, 0:2 * D]) for c in range(2)]))
                finish(product(begin(f"v_{t}")[:, 0:D], [(xT[:, c, tile[t]], wa[:, c, 2 * D:3 * D]) for c in range(2)]))
            pe.wait_ge(qkn_ready, 2 * NT)
            for k, m in enumerate("qk"):
                for c in range(2):
                    a = D * k + 128 * c
                    transposed(f"{m}T{c}", lambda t: qkn[:, t, a:a + 128])
            for m in "qk":
                pe.wait_ge(*done_by(m + "T", 0))
            pe.wait_ge(qkT_dve, 2)
            o = begin("s2")
            for t in range(NT):
                last = product(o[:, tile[t]], [(kT[:, c, tile[t]], qT[:, c, tile[t]]) for c in range(2)])
            finish(last)
            pe.wait_ge(aT_ready, 2)
            pe.wait_ge(v2_ready, NT)
            for c in range(2):
                o = begin(f"oT{c}")
                for t in range(NT):
                    last = pe.matmul(o[:, tile[t]], v2[:, t, 128 * c:128 * c + 128], aT[:, t, :], start=True, stop=True)
                finish(last)
            pe.wait_ge(*done_by("oT", 0))
            pe.wait_ge(oT_dve, 1)
            for t in range(NT):
                finish(product(begin(f"x2_{t}")[:, 0:D], [(oT[:, c, tile[t]], wa[:, c, 3 * D:4 * D]) for c in range(2)]))
            pe.wait_ge(xln_ready, 2 * NT)
            for c in range(2):
                transposed(f"yT{c}", lambda t: xln[:, t, 128 * c:128 * c + 128])
            pe.wait_ge(*done_by("yT", 0))
            pe.wait_ge(xT_dve, 2)
            for k, m in enumerate("qk"):
                for c in range(2):
                    finish(product(begin(f"{m}3_{c}"), [(wf[:, i, D * k + 128 * c:D * k + 128 * c + 128], xT[:, i, :])
                                                        for i in range(2)]))
            pe.wait_ge(diag_ready, 1)
            finish(pe.matmul(begin("gate")[:, 0:NT * NQ], blk, diag.rearrange("p t n -> p (t n)"), start=True, stop=True))
            for b in range(B):
                o = begin(f"v3_{b}")
                for h2 in range(2):
                    last = product(o[64 * h2:64 * h2 + 64, 0:D],
                                   [(xT[:, c, NQ * b:NQ * b + NQ], wf[:, c, 2 * D:3 * D]) for c in range(2)])
                finish(last)
            pe.wait_ge(diag_ready, 2)
            finish(pe.matmul(begin("sel")[:, 0:NT * NQ], blk, diag.rearrange("p t n -> p (t n)"), start=True, stop=True))
            for c in range(2):
                pe.wait_ge(*done_by("q3_", c))
            pe.wait_ge(kblk_act, 8)
            pe.wait_ge(kblk_dve, 8)
            pe.wait_ge(v3_ones, B)
            pe.wait_ge(v3_ready, 2 * B)
            for what, t in ffn_order:
                if what == "s":
                    for c in range(2):
                        o = begin(f"s3_{t}_{c}")
                        for b2 in range(2):
                            a = NQ * (2 * t + b2)
                            last = pe.matmul(o[64 * b2:64 * b2 + 64, :].rearrange("p (h n) -> p h n", h=8),
                                             q3T[:, c, a:a + NQ], kblk[c][:, :, a:a + NQ], start=True, stop=True)
                        finish(last)
                else:
                    pe.wait_ge(p3_ready, t + 1)
                    for c in range(2):
                        transposed(f"pT_{t}_{c}", lambda g: s3[t][:, 8 * c + 2 * g:8 * c + 2 * g + 2, :]
                                   .rearrange("p h n -> p (h n)"), 4)
                    for c in range(2):
                        pe.wait_ge(pTlo_ready, 2 * t + c + 1)
                        o = begin(f"pv_{t}_{c}")
                        for b2 in range(2):
                            rows = slice(64 * b2, 64 * b2 + 64)
                            for q in range(4):
                                g = 4 * c + q
                                v = v3[2 * t + b2][:, g, :]
                                pe.matmul(o[rows, 66 * q:66 * q + 66], pT[t][:, g, rows].bitcast(bf16)[:, 1::2], v,
                                          start=(q == 0), stop=False, skip_group_check=True)
                                last = pe.matmul(o[rows, 66 * q:66 * q + 34], pT_lo[t][:, g, rows], v[:, 0:34],
                                                 start=False, stop=True, skip_group_check=True)
                        finish(last)
            pe.wait_ge(o3_ready, 2 * NT)
            for c in range(2):
                transposed(f"zT{c}", lambda t: o3[:, t, 128 * c:128 * c + 128])
            pe.wait_ge(*done_by("zT", 0))
            pe.wait_ge(zT_dve, 1)
            for t in range(NT):
                finish(product(begin(f"out_{t}")[:, 0:D], [(o3T[:, c, tile[t]], wf[:, c, 3 * D:4 * D]) for c in range(2)]))


def host_constants():
    import numpy as np
    p = np.arange(128)[:, None]
    c = np.arange(128)[None, :]
    parts = [p == c, p // 64 == c // 64, p % 64 == c[:, :64], c[:, :64] < p % 64, p // 16 == c[:, :8],
             64.0 * (p // 64 == c[:, :2]), 64.0 * ((p % 32) // 16 == c[:, :2])]
    return np.concatenate([np.asarray(m, np.float32) for m in parts], axis=1)


def kernel(**inputs):
    import numpy as np
    import concourse.bacc as bacc
    from concourse.bass_utils import run_bass_kernel_spmd

    a = {k: np.asarray(v) for k, v in inputs.items()}
    B, NQ, D = a["x"].shape
    NK = a["ctx_1024"].shape[1]
    w_proj = a["L0_xattn_W_proj"].reshape(8, 2, 16, D).transpose(1, 0, 2, 3).reshape(2, 128, D)
    rows = [a["L0_xattn_b_proj"], a["L0_attn_bq"], a["L0_attn_bk"], a["L0_attn_bv"], a["L0_attn_bo"],
            a["L0_attn_layerscale"], a["L0_ffn_Wg"][:, 0]]
    arrays = {
        "x": a["x"].reshape(B * NQ, D),
        "ctxT": a["ctx_1024"].transpose(0, 2, 1).reshape(B, 2, 128, NK),
        "w_kv": a["L0_xattn_W_kv"],
        "w_q": a["L0_xattn_W_q"],
        "w_proj": w_proj,
        "vecs": np.broadcast_to(np.stack(rows)[None], (128, 7, D)),
        "w_attn": np.concatenate([a["L0_attn_W" + m].T for m in "qkvo"], axis=1),
        "w_ffn": np.concatenate([a["L0_ffn_W" + m] for m in "qkvo"], axis=1),
        "consts": host_constants(),
        "ms_rows": np.full((2, 8 * NK), 4096.0, np.float16),
    }
    nc = bacc.Bacc("TRN2", target_bir_lowering=False, num_devices=1)
    arrays = {k: np.ascontiguousarray(v) for k, v in arrays.items()}
    args = [nc.dram_tensor(k, v.shape, mybir.dt.from_np(v.dtype), kind="ExternalInput").ap() for k, v in arrays.items()]
    out = nc.dram_tensor("out", (B * NQ, D), mybir.dt.float32, kind="ExternalOutput").ap()
    perceiver_layer(nc, *args, out)
    r = run_bass_kernel_spmd(nc, [arrays], core_ids=[0])
    return r.results[0]["out"].reshape(B, NQ, D)
```
